# Optimizing a Trainium2 kernel written in Bass

```python
import numpy as np
import jax
import jax.numpy as jnp

def _softmax(x, axis=-1):
    return jax.nn.softmax(x, axis=axis)

def _gelu(x):
    return jax.nn.gelu(x, approximate=True)

def _silu(x):
    return jax.nn.silu(x)

def _sigmoid(x):
    return jax.nn.sigmoid(x)

def _layernorm(x, axis=-1, eps=1e-05):
    m = jnp.mean(x, axis=axis, keepdims=True)
    v = jnp.var(x, axis=axis, keepdims=True)
    return (x - m) / jnp.sqrt(v + eps)

def _scatter_add(tgt, idx, src, axis=0):
    return tgt.at[idx].add(src)

def _segment_sum(src, seg, n):
    return jax.ops.segment_sum(src, seg, n)
kernel_name = 'mk_cond_resid_d2_seqx_r2_9675d6'

def setup_inputs(seed: int=0):
    np.random.seed(seed)
    _w = jnp.asarray

    def _rec_inputs():
        import jax
        import jax.numpy as jnp
        _rk = jax.random.key(seed)
        x = 7.971e-05 + 1 * jax.random.normal(jax.random.fold_in(_rk, 1), (8, 1024, 512), jnp.float32)
        _lenS = 1024 - jax.random.randint(jax.random.fold_in(_rk, 7), (8,), 0, max(1, 1024 // 4) + 1, jnp.int32)
        _lenS2 = 1024 - jax.random.randint(jax.random.fold_in(_rk, 8), (8,), 0, max(1, 1024 // 4) + 1, jnp.int32)
        itok_B_0_6 = jax.random.randint(jax.random.fold_in(_rk, 11), (8,), 0, 7, jnp.int32)
        itok_B_0_15 = jax.random.randint(jax.random.fold_in(_rk, 12), (8,), 0, 16, jnp.int32)
        return (x, itok_B_0_6, itok_B_0_15)
    x, itok_B_0_6, itok_B_0_15 = _rec_inputs()

    def _L0_cond_setup():
        import jax, jax.numpy as jnp
        import numpy as np
        N_PROFILES = 8
        HIDDEN = 512
        BOTTLENECK = 128
        EPS = 1e-05
        key = jax.random.key(seed)
        ks = jax.random.split(key, 8)
        B, S, H, K, P = (16, 1024, HIDDEN, BOTTLENECK, N_PROFILES)
        down_w = jax.random.normal(ks[0], (P, H, K), dtype=jnp.float32) * (1.0 / np.sqrt(H))
        down_b = jax.random.normal(ks[1], (P, K), dtype=jnp.float32) * 0.01
        up_w = jax.random.normal(ks[2], (P, K, H), dtype=jnp.float32) * (1.0 / np.sqrt(K))
        up_b = jax.random.normal(ks[3], (P, H), dtype=jnp.float32) * 0.01
        ln_g = jnp.ones((P, H), dtype=jnp.float32)
        ln_b = jnp.zeros((P, H), dtype=jnp.float32)
        hidden = jax.random.normal(ks[4], (B, S, H), dtype=jnp.float32)
        profile_ids = jax.random.randint(ks[5], (B,), 0, P)
        return {'hidden': hidden, 'profile_ids': profile_ids, 'down_w': down_w, 'down_b': down_b, 'up_w': up_w, 'up_b': up_b, 'ln_g': ln_g, 'ln_b': ln_b}
    _L0_cond_all = _L0_cond_setup()
    _L0_cond_in = {k: v for k, v in _L0_cond_all.items() if k in ('down_w', 'down_b', 'up_w', 'up_b', 'ln_g', 'ln_b')}
    del _L0_cond_all

    def _L1_cond_setup():
        import jax, jax.numpy as jnp
        import numpy as np
        B, N, DIM = (32, 512, 512)
        HID = 2048
        PART = 128
        OUT = 512
        SHARED = OUT - PART
        E = 16
        key = jax.random.key(seed)
        ks = jax.random.split(key, 8)
        s = 0.02
        return {'x': jax.random.normal(ks[0], (B, N, DIM), dtype=jnp.float32), 'indices': jax.random.randint(ks[1], (B,), 0, E, dtype=jnp.int64), 'fc1_w': jax.random.normal(ks[2], (HID, DIM), dtype=jnp.float32) * s, 'fc1_b': jnp.zeros((HID,), dtype=jnp.float32), 'fc2_w': jax.random.normal(ks[3], (SHARED, HID), dtype=jnp.float32) * s, 'fc2_b': jnp.zeros((SHARED,), dtype=jnp.float32), 'experts_w': jax.random.normal(ks[4], (E, PART, HID), dtype=jnp.float32) * s, 'experts_b': jnp.zeros((E, PART), dtype=jnp.float32)}
    _L1_cond_all = _L1_cond_setup()
    _L1_cond_in = {k: v for k, v in _L1_cond_all.items() if k in ('fc1_w', 'fc1_b', 'fc2_w', 'fc2_b', 'experts_w', 'experts_b')}
    del _L1_cond_all
    return {'x': x, 'itok_B_0_6': itok_B_0_6, 'itok_B_0_15': itok_B_0_15, 'L0_cond_down_w': _L0_cond_in['down_w'], 'L0_cond_down_b': _L0_cond_in['down_b'], 'L0_cond_up_w': _L0_cond_in['up_w'], 'L0_cond_up_b': _L0_cond_in['up_b'], 'L0_cond_ln_g': _L0_cond_in['ln_g'], 'L0_cond_ln_b': _L0_cond_in['ln_b'], 'L1_cond_fc1_w': _L1_cond_in['fc1_w'], 'L1_cond_fc1_b': _L1_cond_in['fc1_b'], 'L1_cond_fc2_w': _L1_cond_in['fc2_w'], 'L1_cond_fc2_b': _L1_cond_in['fc2_b'], 'L1_cond_experts_w': _L1_cond_in['experts_w'], 'L1_cond_experts_b': _L1_cond_in['experts_b']}

def reference(x, itok_B_0_6, itok_B_0_15, L0_cond_down_w, L0_cond_down_b, L0_cond_up_w, L0_cond_up_b, L0_cond_ln_g, L0_cond_ln_b, L1_cond_fc1_w, L1_cond_fc1_b, L1_cond_fc2_w, L1_cond_fc2_b, L1_cond_experts_w, L1_cond_experts_b):
    import jax
    import jax.numpy as jnp

    def _L0_cond_ref(hidden, profile_ids, down_w, down_b, up_w, up_b, ln_g, ln_b):
        import jax, jax.numpy as jnp
        import numpy as np
        N_PROFILES = 8
        HIDDEN = 512
        BOTTLENECK = 128
        EPS = 1e-05
        Wd = down_w[profile_ids]
        bd = down_b[profile_ids][:, None]
        Wu = up_w[profile_ids]
        bu = up_b[profile_ids][:, None]
        g = ln_g[profile_ids][:, None]
        b = ln_b[profile_ids][:, None]
        z = jax.nn.relu(jnp.einsum('bsh,bhk->bsk', hidden, Wd) + bd)
        y = hidden + jnp.einsum('bsk,bkh->bsh', z, Wu) + bu
        mu = jnp.mean(y, axis=-1, keepdims=True)
        var = jnp.mean(jnp.square(y - mu), axis=-1, keepdims=True)
        return (y - mu) * jax.lax.rsqrt(var + EPS) * g + b

    def _L1_cond_ref(x, indices, fc1_w, fc1_b, fc2_w, fc2_b, experts_w, experts_b):
        import jax, jax.numpy as jnp
        import numpy as np
        B, N, DIM = (32, 512, 512)
        HID = 2048
        PART = 128
        OUT = 512
        SHARED = OUT - PART
        E = 16
        h = jax.nn.gelu(jnp.einsum('bnd,hd->bnh', x, fc1_w) + fc1_b, approximate=False)
        shared = jnp.einsum('bnh,sh->bns', h, fc2_w) + fc2_b
        We = experts_w[indices]
        be = experts_b[indices]
        expert_x = jnp.einsum('bnh,bph->bnp', h, We) + be[:, None, :]
        return jnp.concatenate([shared, expert_x], axis=-1)
    x = x + _L0_cond_ref(x, itok_B_0_6, L0_cond_down_w, L0_cond_down_b, L0_cond_up_w, L0_cond_up_b, L0_cond_ln_g, L0_cond_ln_b)
    x = x + _L1_cond_ref(x, itok_B_0_15, L1_cond_fc1_w, L1_cond_fc1_b, L1_cond_fc2_w, L1_cond_fc2_b, L1_cond_experts_w, L1_cond_experts_b)
    return x

_drawn_inputs = setup_inputs


def setup_inputs(seed=0):
    import zlib

    import numpy as np

    out = dict(_drawn_inputs(seed))
    spreads = {'L0_cond_ln_g': (1.0, 0.2),
     'L0_cond_ln_b': (0.0, 0.1),
     'L1_cond_fc1_b': (0.0, 0.271),
     'L1_cond_fc2_b': (0.0, 0.1),
     'L1_cond_experts_b': (0.0, 0.339)}
    factors = {'L0_cond_down_b': 8.0, 'L0_cond_up_b': 8.0}
    for name, (base, spread) in spreads.items():
        noise = np.random.default_rng([zlib.crc32(name.encode()), seed]).standard_normal(out[name].shape)
        drawn = base * np.exp(spread * noise) if base else spread * noise
        out[name] = jnp.asarray(drawn.astype(out[name].dtype))
    for name, factor in factors.items():
        out[name] = (out[name] * factor).astype(out[name].dtype)
    return out
```

```python
import concourse.bass as bass
from concourse import mybir
from contextlib import ExitStack

P = 128
BATCH, SEQ, D = 8, 1024, 512
NPROF, NEXP = 8, 16
HID, SHARED = 2048, 384
TB = 512
NBLK = BATCH * SEQ // TB
PER_SEQ = SEQ // TB
C = D // P
T = TB // P
J = HID // P
LAG = 2
PIECE = 512
STAGES = 6
W1_PIECES = HID * D // P // PIECE
W2_PIECES = HID * SHARED // P // PIECE
EXP_PIECES = HID * (D - SHARED) // P // PIECE
JQ = J // EXP_PIECES
EPS = 1e-5

XSPLIT_AT = {3: (0, 1), 5: (2,), 6: (3,)}
DOWN_AT = {4: (0,), 5: (1,), 6: (2,), 7: (3,)}
Z_AT = 8
UP_AT = {9: (0, 1), 10: (2, 3)}
Y_AT = {9: (0, 1), 10: (2, 3)}
RSTD_AT = 10
NORM_AT = 11
TRANSPOSE_AT = {13: (0, 1), 14: (2, 3)}
X1_AT = {13: (0, 1), 14: (2, 3)}
PROFILE_AT = J - 1
EXPERT_AT = {6: 0, 10: 1, 14: 2}

AHEAD = 3


def _first_pieces():
    order = {-1: [("down", 0), ("up", 0)] + [("w1", n) for n in range(AHEAD)] + [("exp", 0), ("w2", 0)]}
    sent = 1
    for j in range(J):
        order[j] = [("w1", j + AHEAD)] if j + AHEAD < J else []
        if j % JQ == 2 and j // JQ + 1 < EXP_PIECES:
            order[j].append(("exp", j // JQ + 1))
        while sent * PIECE < min(j + 2, J) * SHARED:
            order[j].append(("w2", sent))
            sent += 1
    return order


FIRST_PIECES = _first_pieces()
FIRST_INDEX = {}
for _step in range(-1, J):
    for _item in FIRST_PIECES[_step]:
        FIRST_INDEX[_item] = len(FIRST_INDEX)
N_FIRST = len(FIRST_INDEX)
NEXT_ORDER = [("down", 0), ("up", 0), ("exp", 0), ("exp", 1), ("exp", 2), ("exp", 3)]


def build(nc, x, x_t, itok_prof, itok_exp, down_w, up_w, prof_vecs, up_b, w1, w2, exp_w,
          exp_b, const_vecs, out_t):
    fp32, fp32r = mybir.dt.float32, mybir.dt.float32r
    ALU, ACT = mybir.AluOpType, mybir.ActivationFunctionType
    ctx = ExitStack()
    with ctx:
        def sb(name, shape, dt=fp32):
            return ctx.enter_context(nc.sbuf_tensor(name, shape, dt))

        def sem(name):
            return ctx.enter_context(nc.semaphore(name))

        w1_s = sb("w1_s", [P, 2, J * C * P], fp32r)
        w2_s = sb("w2_s", [P, 2, J * SHARED], fp32r)
        exp_s = sb("exp_s", [P, 2, J * P], fp32r)
        down_s = sb("down_s", [P, 2, C * P], fp32r)
        up_s = sb("up_s", [P, 2, D], fp32r)
        stage = sb("stage", [P, STAGES, PIECE])
        x_rows = sb("x_rows", [P, T, D])
        x_cols = sb("x_cols", [P, PER_SEQ, C, TB])
        xs = sb("xs", [P, 2, 2, TB], fp32r)
        x1_s = sb("x1_s", [P, 2, C, TB], fp32r)
        z_raw = sb("z_raw", [P, TB])
        h_raw = sb("h_raw", [P, 2, TB])
        h_s = sb("h_s", [P, 3, 2, TB], fp32r)
        prof_v = sb("prof_v", [P, 1 + 2 * C])
        bup = sb("bup", [P, D])
        const_v = sb("const_v", [P, J + SHARED // P])
        exp_v = sb("exp_v", [P, 1])
        ident = sb("ident", [P, P])
        stats = sb("stats", [P, T, 6])
        mean_var = sb("mean_var", [P, T, 2])
        var_eps = sb("var_eps", [P, T])
        rstd = sb("rstd", [P, T])
        neg_half = sb("neg_half", [P, T])
        eps = sb("eps", [P, T])
        warm = sb("warm", [P, 2])

        acc = [ctx.enter_context(nc.psum_tensor(f"acc{o}", [P, TB], fp32)) for o in range(C)]
        hid = [ctx.enter_context(nc.psum_tensor(f"hid{k}", [P, TB], fp32)) for k in range(2)]
        bank_a = ctx.enter_context(nc.psum_tensor("bank_a", [P, TB], fp32))
        bank_b = ctx.enter_context(nc.psum_tensor("bank_b", [P, TB], fp32))
        UP_BANK = [bank_b, bank_a, bank_b, bank_a]
        TR_BANK = [bank_b, bank_a, bank_b, bank_a]

        x_loaded, const_loaded = sem("x_loaded"), sem("const_loaded")
        xt_loaded = [sem(f"xt_loaded{c}") for c in range(C)]
        prof_loaded, exp_v_loaded = sem("prof_loaded"), sem("exp_v_loaded")
        stage_loaded = [sem(f"stage_loaded{s}") for s in range(STAGES)]
        out_stored = [sem(f"out_stored{o}") for o in range(C)]
        stage_hi, stage_split = sem("stage_hi"), sem("stage_split")
        const_set, ident_ready = sem("const_set"), sem("ident_ready")
        xb_ready, x_hi, x_split, xtb_ready = sem("xb_ready"), sem("x_hi"), sem("x_split"), sem("xtb_ready")
        down_done, z_done, z_hi, z_split = sem("down_done"), sem("z_done"), sem("z_hi"), sem("z_split")
        up_done, y_done, stats_done, aggr_done = sem("up_done"), sem("y_done"), sem("stats_done"), sem("aggr_done")
        stats_seen, warm_set = sem("stats_seen"), sem("warm_set")
        var_done, rstd_done, norm_done, tr_done = sem("var_done"), sem("rstd_done"), sem("norm_done"), sem("tr_done")
        x1_done, x1_hi, x1_split = sem("x1_done"), sem("x1_hi"), sem("x1_split")
        fc1_done, gelu_done, h_hi, h_split = sem("fc1_done"), sem("gelu_done"), sem("h_hi"), sem("h_split")
        fc2_done, acc_done, out_ready = sem("fc2_done"), sem("acc_done"), sem("out_ready")

        block = ctx.enter_context(nc.Block())

        def wait(eng, s, value):
            if not isinstance(value, int) or value > 0:
                eng.wait_ge(s, value)

        def plain(ap):
            return ap.bitcast(fp32)

        def piece_dst(kind, n, half):
            tensor = {"w1": w1_s, "w2": w2_s, "exp": exp_s, "down": down_s, "up": up_s}[kind]
            return tensor[:, half, n * PIECE:(n + 1) * PIECE]

        def next_index(m, v, seq0):
            return N_FIRST + len(NEXT_ORDER) * (seq0 - 1) + m + (len(NEXT_ORDER) * v if not isinstance(v, int) or v else 0)

        def stage_slot(m, seq0):
            return (N_FIRST + len(NEXT_ORDER) * (seq0 - 1) + m) % STAGES

        assert len(NEXT_ORDER) == STAGES

        def stage_uses(m, v, seq0):
            return (N_FIRST + len(NEXT_ORDER) * (seq0 - 1) + m) // STAGES + 1 + v

        def counter(v, seq0, q):
            def count(per, n, shift=0):
                fixed = per * (PER_SEQ * seq0 + q + shift) + n
                return fixed + v * (per * PER_SEQ) if not isinstance(v, int) else fixed
            return count

        @block.sync
        def _(sp):
            def load_piece(kind, n, slot, uses, src):
                sp.dma_start(stage[:, slot, :], src).then_inc(stage_loaded[slot], 16)

            def source(kind, n, prof=None, expert=None):
                if kind == "w1":
                    return w1[:, n * PIECE:(n + 1) * PIECE]
                if kind == "w2":
                    return w2[:, n * PIECE:(n + 1) * PIECE]
                if kind == "exp":
                    return exp_w[bass.ds(expert, 1), :, n * PIECE:(n + 1) * PIECE].rearrange("e p n -> (e p) n")
                w = down_w if kind == "down" else up_w
                return w[bass.ds(prof, 1), :, :].rearrange("e p n -> (e p) n")

            def load_first(item):
                k = FIRST_INDEX[item]
                wait(sp, stage_split, k + 1 - STAGES)
                load_piece(*item, k % STAGES, 0, source(*item, prof0, expert0))

            def load_next(m, v, seq0, prof, expert):
                wait(sp, stage_split, next_index(m, v, seq0) + 1 - STAGES)
                load_piece(*NEXT_ORDER[m], stage_slot(m, seq0), 0, source(*NEXT_ORDER[m], prof, expert))

            def load_profile(prof):
                sp.dma_start(prof_v[:], prof_vecs[bass.ds(prof, 1), :, :].rearrange("e p n -> (e p) n")).then_inc(prof_loaded, 16)
                sp.dma_start(bup[:], up_b[bass.ds(prof, 1), :].to_broadcast([P, D])).then_inc(prof_loaded, 16)

            def chosen(itok, n, most):
                return sp.value_load(itok[0:1, bass.ds(n, 1)], min_val=0, max_val=most)

            def block_rows(blk):
                return x[bass.ds(blk, 1), :, :].rearrange("b p n -> (b p) n").rearrange("p (t d) -> p t d", t=T)

            def block_cols(tensor, blk, c):
                return tensor[bass.ds(blk, 1), :, c, :].rearrange("b p n -> (b p) n")

            sp.dma_start(x_cols[:, 0, 0, :], block_cols(x_t, 0, 0)).then_inc(xt_loaded[0], 16)
            prof0 = chosen(itok_prof, 0, NPROF - 1)
            load_piece("down", 0, 0, 0, source("down", 0, prof0))
            load_piece("up", 0, 1, 0, source("up", 0, prof0))
            load_profile(prof0)
            expert0 = chosen(itok_exp, 0, NEXP - 1)
            for item in FIRST_PIECES[-1][2:]:
                load_first(item)
            sp.dma_start(exp_v[:], exp_b[bass.ds(expert0, 1), :, :].rearrange("e p n -> (e p) n")).then_inc(exp_v_loaded, 16)

            def one_block(v, seq0, q, first, last, ids):
                count = counter(v, seq0, q)
                start = first and q == 0
                more = not (last and q == PER_SEQ - 1)
                blk = PER_SEQ * (seq0 + v) + q
                if q == 0:
                    ids["expert"] = chosen(itok_exp, seq0 + v, NEXP - 1) if not first else expert0
                    if not last:
                        ids["next_prof"] = chosen(itok_prof, seq0 + 1 + v, NPROF - 1)
                        ids["next_expert"] = chosen(itok_exp, seq0 + 1 + v, NEXP - 1)
                if more:
                    sp.wait_ge(tr_done, count(C, 0, 1))
                    sp.dma_start(x_rows[:], block_rows(blk + 1)).then_inc(x_loaded, 16)
                if not start:
                    for o in range(C):
                        sp.wait_ge(out_ready, count(C, o + 1, -1))
                        sp.dma_start(block_cols(out_t, blk - 1, o), x_cols[:, (q + 1) % 2, o, :]).then_inc(out_stored[o], 16)
                if more:
                    for c in range(C):
                        if not start:
                            sp.wait_ge(out_stored[c], count(16, 0))
                        sp.dma_start(x_cols[:, (q + 1) % 2, c, :], block_cols(x_t, blk + 1, c)).then_inc(xt_loaded[c], 16)
                if q == 0 and not first:
                    sp.dma_start(exp_v[:], exp_b[bass.ds(ids["expert"], 1), :, :].rearrange("e p n -> (e p) n")).then_inc(exp_v_loaded, 16)
                if start:
                    for j in range(J):
                        for item in FIRST_PIECES[j]:
                            load_first(item)
                if not last:
                    for m in (range(5) if q == 0 else (5,)):
                        load_next(m, v, seq0 + 1, ids["next_prof"], ids["next_expert"])
                    if q == 0:
                        sp.wait_ge(x1_done, count(C, 0, 2))
                        load_profile(ids["next_prof"])

            def sequence(v, seq0, first=False, last=False):
                ids = {}
                for q in range(PER_SEQ):
                    one_block(v, seq0, q, first, last, ids)

            sequence(0, 0, first=True)
            with sp.Fori(0, BATCH - 2) as v:
                sequence(v, 1)
            sequence(0, BATCH - 1, last=True)
            for o in range(C):
                sp.wait_ge(out_ready, C * (NBLK - 1) + o + 1)
                sp.dma_start(block_cols(out_t, NBLK - 1, o), x_cols[:, (NBLK - 1) % 2, o, :]).then_inc(out_stored[o], 16)
            for o in range(C):
                sp.wait_ge(out_stored[o], 16 * NBLK)

        @block.tensor
        def _(pe):
            def three(out, w_hi, w_lo, m_hi, m_lo, start, stop):
                nc.tensor.matmul(out, w_hi, m_hi, start=start, stop=False)
                nc.tensor.matmul(out, w_hi, m_lo, start=False, stop=False)
                return nc.tensor.matmul(out, w_lo, m_hi, start=False, stop=stop)

            def down(count, shift, c, weights, x_hi_lo=None):
                if c == 0:
                    wait(pe, x1_done, count(C, 0, shift))
                    if weights is not None:
                        pe.wait_ge(stage_split, weights)
                pe.wait_ge(x_split, count(C, c + 1, shift))
                k = slice(c * P, (c + 1) * P)
                part = x_hi_lo or (xs[:, c % 2, 0, :], xs[:, c % 2, 1, :])
                three(bank_a[:], down_s[:, 0, k], down_s[:, 1, k], *part, c == 0, c == C - 1).then_inc(down_done, 1)

            def up(count, shift, t, weights):
                if t == 0:
                    pe.wait_ge(z_split, count(1, 1, shift))
                    if weights is not None:
                        pe.wait_ge(stage_split, weights)
                if t >= 2:
                    pe.wait_ge(y_done, count(T, t - 1, shift))
                k = slice(t * P, (t + 1) * P)
                three(UP_BANK[t][:], xs[:, 0, 0, k], xs[:, 0, 1, k], up_s[:, 0, :], up_s[:, 1, :],
                      True, True).then_inc(up_done, 1)

            def transpose(count, shift, c):
                if c == 0:
                    pe.wait_ge(norm_done, count(T, T, shift))
                if c >= 2:
                    pe.wait_ge(x1_done, count(C, c - 1, shift))
                for t in range(T):
                    ins = nc.tensor.transpose(TR_BANK[c][:, t * P:(t + 1) * P],
                                              x_rows[:, t, c * P:(c + 1) * P], ident[:])
                ins.then_inc(tr_done, 1)

            def fc1(count, j, start_block):
                wait(pe, gelu_done, count(J, j - 1))
                if start_block:
                    pe.wait_ge(stage_split, FIRST_INDEX[("w1", j)] + 1)
                for c in range(C):
                    if j == 0:
                        pe.wait_ge(x1_split, count(C, c + 1))
                    k = slice((j * C + c) * P, (j * C + c + 1) * P)
                    ins = three(hid[j % 2][:], w1_s[:, 0, k], w1_s[:, 1, k], x1_s[:, 0, c, :], x1_s[:, 1, c, :],
                                c == 0, c == C - 1)
                ins.then_inc(fc1_done, 1)

            def fc2(count, j, start_block, weights):
                pe.wait_ge(h_split, count(J, j + 1))
                if start_block:
                    last = (("w2", ((j + 1) * SHARED - 1) // PIECE), ("exp", j // JQ))
                    pe.wait_ge(stage_split, max(FIRST_INDEX[i] for i in last) + 1)
                elif weights is not None and j % JQ == 0:
                    pe.wait_ge(stage_split, weights[j // JQ])
                for o in range(C):
                    if j == 0:
                        wait(pe, out_ready, count(C, o + 1, -1))
                    if o < SHARED // P:
                        k = slice(j * SHARED + o * P, j * SHARED + (o + 1) * P)
                        w_hi, w_lo = w2_s[:, 0, k], w2_s[:, 1, k]
                    else:
                        k = slice(j * P, (j + 1) * P)
                        w_hi, w_lo = exp_s[:, 0, k], exp_s[:, 1, k]
                    ins = three(acc[o][:], w_hi, w_lo, h_s[:, j % 3, 0, :], h_s[:, j % 3, 1, :], j == 0, j == J - 1)
                    if j == J - 1:
                        ins.then_inc(acc_done, 1)
                if j < J - 1:
                    ins.then_inc(fc2_done, 1)

            zero = counter(0, 0, 0)
            for c in range(C):
                down(zero, 0, c, FIRST_INDEX[("down", 0)] + 1, (x1_s[:, 0, c, :], x1_s[:, 1, c, :]))
            for t in range(T):
                up(zero, 0, t, FIRST_INDEX[("up", 0)] + 1)
            pe.wait_ge(ident_ready, 1)
            for c in range(C):
                transpose(zero, 0, c)

            def sequence(v, seq0, first=False, last=False):
                for q in range(PER_SEQ):
                    count = counter(v, seq0, q)
                    start_block = first and q == 0
                    more = not (last and q == PER_SEQ - 1)
                    new_profile = more and q == PER_SEQ - 1
                    down_w_at = next_index(0, v, seq0 + 1) + 1 if new_profile else None
                    up_w_at = next_index(1, v, seq0 + 1) + 1 if new_profile else None
                    exp_at = [next_index(2 + n, v, seq0) + 1 for n in range(EXP_PIECES)] if q == 0 and not first else None
                    for j in range(J):
                        fc1(count, j, start_block)
                        if j >= LAG:
                            fc2(count, j - LAG, start_block, exp_at)
                        if more:
                            for c in DOWN_AT.get(j, ()):
                                down(count, 1, c, down_w_at)
                            for t in UP_AT.get(j, ()):
                                up(count, 1, t, up_w_at)
                            for c in TRANSPOSE_AT.get(j, ()):
                                transpose(count, 1, c)
                    for j in range(J - LAG, J):
                        fc2(count, j, start_block, exp_at)

            sequence(0, 0, first=True)
            with pe.Fori(0, BATCH - 2) as v:
                sequence(v, 1)
            sequence(0, BATCH - 1, last=True)

        @block.scalar
        def _(act):
            def piece_hi(kind, n, slot, uses):
                act.wait_ge(stage_loaded[slot], uses * 16)
                nc.scalar.activation(piece_dst(kind, n, 0), stage[:, slot, :], ACT.Copy).then_inc(stage_hi, 1)

            def first_hi(item):
                k = FIRST_INDEX[item]
                piece_hi(*item, k % STAGES, k // STAGES + 1)

            def next_hi(m, v, seq0):
                piece_hi(*NEXT_ORDER[m], stage_slot(m, seq0), stage_uses(m, v, seq0))

            def split_x(count, shift, q, c):
                act.wait_ge(xt_loaded[c], count(16, 16, shift))
                if c == 0:
                    wait(act, up_done, count(T, 0, shift))
                elif c == 1:
                    wait(act, down_done, count(C, 0, shift))
                else:
                    act.wait_ge(down_done, count(C, c - 1, shift))
                nc.scalar.activation(xs[:, c % 2, 0, :], x_cols[:, q, c, :], ACT.Copy).then_inc(x_hi, 1)

            def relu_z(count, shift):
                act.wait_ge(down_done, count(C, C, shift))
                wait(act, z_split, count(1, 0, shift))
                nc.scalar.activation(z_raw[:], bank_a[:], ACT.Relu, bias=prof_v[:, 0:1]).then_inc(z_done, 1)

            def split_x1(count, shift, q):
                for c in range(C):
                    act.wait_ge(x1_done, count(C, c + 1, shift))
                    nc.scalar.activation(x1_s[:, 0, c, :], x_cols[:, q, c, :], ACT.Copy).then_inc(x1_hi, 1)

            for c in range(1, C):
                act.dma_start(x_cols[:, 0, c, :], x_t[0, :, c, :]).then_inc(xt_loaded[c], 16)
            act.dma_start(x_rows[:], x[0, :, :].rearrange("p (t d) -> p t d", t=T)).then_inc(x_loaded, 16)
            act.dma_start(const_v[:], const_vecs).then_inc(const_loaded, 16)
            act.wait_ge(warm_set, 1)
            nc.scalar.activation(warm[:, 1:2], warm[:, 0:1], ACT.Gelu)
            zero = counter(0, 0, 0)
            first_hi(("down", 0))
            for c in range(C):
                act.wait_ge(xt_loaded[c], 16)
                nc.scalar.activation(x1_s[:, 0, c, :], x_cols[:, 0, c, :], ACT.Copy).then_inc(x_hi, 1)
            first_hi(("up", 0))
            act.wait_ge(prof_loaded, 32)
            relu_z(zero, 0)
            for item in FIRST_PIECES[-1][2:]:
                first_hi(item)
            act.wait_ge(const_loaded, 16)
            split_x1(zero, 0, 0)

            def sequence(v, seq0, first=False, last=False):
                for q in range(PER_SEQ):
                    count = counter(v, seq0, q)
                    more = not (last and q == PER_SEQ - 1)
                    for j in range(J):
                        act.wait_ge(fc1_done, count(J, j + 1))
                        wait(act, h_split, count(J, j - 1))
                        nc.scalar.activation(h_raw[:, j % 2, :], hid[j % 2][:], ACT.Gelu,
                                             bias=const_v[:, j:j + 1]).then_inc(gelu_done, 1)
                        if first and q == 0:
                            for item in FIRST_PIECES[j]:
                                first_hi(item)
                        if j == 0 and q == 0 and not first:
                            act.wait_ge(acc_done, count(C, 0))
                            next_hi(5, v, seq0)
                        if not more:
                            continue
                        for c in XSPLIT_AT.get(j, ()):
                            split_x(count, 1, (q + 1) % 2, c)
                        if j == Z_AT:
                            if q == PER_SEQ - 1:
                                act.wait_ge(prof_loaded, 32 * (seq0 + 2) + (32 * v if not isinstance(v, int) else 0))
                            relu_z(count, 1)
                        if q == 0 and not last and j == PROFILE_AT:
                            act.wait_ge(down_done, count(C, 0, 2))
                            next_hi(0, v, seq0 + 1)
                            act.wait_ge(up_done, count(T, 0, 2))
                            next_hi(1, v, seq0 + 1)
                        if q == PER_SEQ - 1 and j in EXPERT_AT:
                            n = EXPERT_AT[j]
                            act.wait_ge(fc2_done, count(J - 1, (n + 1) * JQ))
                            next_hi(2 + n, v, seq0 + 1)
                    if more:
                        split_x1(count, 1, (q + 1) % 2)

            sequence(0, 0, first=True)
            with act.Fori(0, BATCH - 2) as v:
                sequence(v, 1)
            sequence(0, BATCH - 1, last=True)

        @block.vector
        def _(dve):
            def split_x(count, shift, q, c):
                dve.wait_ge(x_hi, count(C, c + 1, shift))
                nc.vector.tensor_tensor(xs[:, c % 2, 1, :], x_cols[:, q, c, :], plain(xs[:, c % 2, 0, :]),
                                        ALU.subtract).then_inc(x_split, 1)

            def split_z(count, shift):
                dve.wait_ge(z_done, count(1, 1, shift))
                nc.vector.tensor_copy(xs[:, 0, 0, :], z_raw[:]).then_inc(z_hi, 1)
                dve.wait_ge(z_hi, count(1, 1, shift))
                nc.vector.tensor_tensor(xs[:, 0, 1, :], z_raw[:], plain(xs[:, 0, 0, :]),
                                        ALU.subtract).then_inc(z_split, 1)

            def residual_stats(count, shift, t):
                if t == 0:
                    dve.wait_ge(xb_ready, count(1, 1, shift))
                dve.wait_ge(up_done, count(T, t + 1, shift))
                nc.vector.tensor_tensor(x_rows[:, t, :], UP_BANK[t][:], x_rows[:, t, :], ALU.add).then_inc(y_done, 1)
                dve.wait_ge(y_done, count(T, t + 1, shift))
                nc.vector.bn_stats(stats[:, t, :], x_rows[:, t, :]).then_inc(stats_done, 1)
                dve.wait_ge(stats_done, count(T, t + 1, shift))
                dve.sem_inc(stats_seen)
                nc.vector.bn_aggr(mean_var[:, t, :], stats[:, t, :]).then_inc(aggr_done, 1)

            def norm(count, shift):
                dve.wait_ge(rstd_done, count(1, 1, shift))
                for t in range(T):
                    nc.vector.tensor_scalar(x_rows[:, t, :], x_rows[:, t, :], mean_var[:, t, 0:1], rstd[:, t:t + 1],
                                            ALU.subtract, ALU.mult).then_inc(norm_done, 1)

            def make_x1(count, shift, q, c):
                dve.wait_ge(tr_done, count(C, c + 1, shift))
                dve.wait_ge(xtb_ready, count(C, c + 1, shift))
                nc.vector.scalar_tensor_tensor(out=x_cols[:, q, c, :], in0=TR_BANK[c][:], scalar=prof_v[:, 1 + c:2 + c],
                                               in1=x_cols[:, q, c, :], op0=ALU.mult, op1=ALU.add).then_inc(x1_done, 1)

            def split_x1(count, shift, q, c):
                dve.wait_ge(x1_hi, count(C, c + 1, shift))
                nc.vector.tensor_tensor(x1_s[:, 1, c, :], x_cols[:, q, c, :], plain(x1_s[:, 0, c, :]),
                                        ALU.subtract).then_inc(x1_split, 1)

            zero = counter(0, 0, 0)
            nc.vector.memset(warm[:], 0.0).then_inc(warm_set, 1)
            dve.wait_ge(stage_hi, 1)
            nc.vector.tensor_tensor(down_s[:, 1, :], stage[:, 0, :], plain(down_s[:, 0, :]),
                                    ALU.subtract).then_inc(stage_split, 1)
            for c in range(C):
                dve.wait_ge(x_hi, c + 1)
                nc.vector.tensor_tensor(x1_s[:, 1, c, :], x_cols[:, 0, c, :], plain(x1_s[:, 0, c, :]),
                                        ALU.subtract).then_inc(x_split, 1)
            dve.wait_ge(x_loaded, 16)
            dve.wait_ge(prof_loaded, 32)
            for t in range(T):
                ins = nc.vector.tensor_tensor(x_rows[:, t, :], x_rows[:, t, :], bup[:], ALU.add)
            ins.then_inc(xb_ready, 1)
            split_z(zero, 0)
            for t in range(T):
                residual_stats(zero, 0, t)
            norm(zero, 0)
            make_x1(zero, 0, 0, 0)
            for c in range(C):
                if c + 1 < C:
                    make_x1(zero, 0, 0, c + 1)
                split_x1(zero, 0, 0, c)
            dve.wait_ge(const_loaded, 16)

            def sequence(v, seq0, first=False, last=False):
                for q in range(PER_SEQ):
                    count = counter(v, seq0, q)
                    more = not (last and q == PER_SEQ - 1)
                    for j in range(J):
                        dve.wait_ge(gelu_done, count(J, j + 1))
                        if j >= 3:
                            dve.wait_ge(fc2_done, count(J - 1, j - 2))
                        hi, lo = h_s[:, j % 3, 0, :], h_s[:, j % 3, 1, :]
                        nc.vector.tensor_copy(hi, h_raw[:, j % 2, :]).then_inc(h_hi, 1)
                        dve.wait_ge(h_hi, count(J, j + 1))
                        nc.vector.tensor_tensor(lo, h_raw[:, j % 2, :], plain(hi), ALU.subtract).then_inc(h_split, 1)
                        if not more:
                            continue
                        for c in XSPLIT_AT.get(j, ()):
                            split_x(count, 1, (q + 1) % 2, c)
                        if j == Z_AT:
                            split_z(count, 1)
                        for t in Y_AT.get(j, ()):
                            residual_stats(count, 1, t)
                        if j == NORM_AT:
                            norm(count, 1)
                        for c in X1_AT.get(j, ()):
                            make_x1(count, 1, (q + 1) % 2, c)
                    if more:
                        for c in range(C):
                            split_x1(count, 1, (q + 1) % 2, c)
                    if q == 0:
                        dve.wait_ge(exp_v_loaded, 16 * (seq0 + 1) + (16 * v if not isinstance(v, int) else 0))
                    for o in range(C):
                        bias = const_v[:, J + o:J + o + 1] if o < SHARED // P else exp_v[:]
                        dve.wait_ge(acc_done, count(C, o + 1))
                        nc.vector.scalar_tensor_tensor(out=x_cols[:, q, o, :], in0=acc[o][:], scalar=bias,
                                                       in1=x_cols[:, q, o, :], op0=ALU.add, op1=ALU.add).then_inc(out_ready, 1)

            sequence(0, 0, first=True)
            with dve.Fori(0, BATCH - 2) as v:
                sequence(v, 1)
            sequence(0, BATCH - 1, last=True)

        @block.gpsimd
        def _(pool):
            def piece_lo(kind, n, slot, index):
                pool.wait_ge(stage_hi, index + 1)
                nc.gpsimd.tensor_tensor(piece_dst(kind, n, 1), stage[:, slot, :], plain(piece_dst(kind, n, 0)),
                                        ALU.subtract).then_inc(stage_split, 1)

            def first_lo(item):
                k = FIRST_INDEX[item]
                piece_lo(*item, k % STAGES, k)

            def next_lo(m, v, seq0):
                piece_lo(*NEXT_ORDER[m], stage_slot(m, seq0), next_index(m, v, seq0))

            def add_up_bias(count, shift):
                pool.wait_ge(x_loaded, count(16, 16, shift))
                nc.gpsimd.tensor_tensor(x_rows[:], x_rows[:], bup[:].unsqueeze(1).to_broadcast([P, T, D]),
                                        ALU.add).then_inc(xb_ready, 1)

            def add_norm_bias(count, shift, q, c):
                pool.wait_ge(x_split, count(C, c + 1, shift))
                nc.gpsimd.tensor_tensor(x_cols[:, q, c, :], x_cols[:, q, c, :],
                                        prof_v[:, 1 + C + c:2 + C + c].to_broadcast([P, TB]),
                                        ALU.add).then_inc(xtb_ready, 1)

            def make_rstd(count, shift):
                pool.wait_ge(aggr_done, count(T, T, shift))
                wait(pool, norm_done, count(T, 0, shift))
                nc.gpsimd.tensor_tensor(var_eps[:], mean_var[:, :, 1], eps[:], ALU.add).then_inc(var_done, 1)
                pool.wait_ge(var_done, count(1, 1, shift))
                nc.gpsimd.tensor_tensor(rstd[:], var_eps[:], neg_half[:], ALU.pow).then_inc(rstd_done, 1)

            nc.gpsimd.memset(neg_half[:], -0.5).then_inc(const_set, 1)
            nc.gpsimd.memset(eps[:], EPS).then_inc(const_set, 1)
            nc.gpsimd.memset(ident[:], 0.0).then_inc(const_set, 1)
            pool.wait_ge(const_set, 3)
            nc.gpsimd.affine_select(out=ident[:], in_=ident[:], compare_op=ALU.not_equal, fill=1.0, base=0,
                                    pattern=[[-1, P]], channel_multiplier=1).then_inc(ident_ready, 1)
            pool.wait_ge(stage_split, 1)
            first_lo(("up", 0))
            zero = counter(0, 0, 0)
            pool.wait_ge(prof_loaded, 32)
            for c in range(C):
                add_norm_bias(zero, 0, 0, c)
            for item in FIRST_PIECES[-1][2:4]:
                first_lo(item)
            make_rstd(zero, 0)
            for item in FIRST_PIECES[-1][4:]:
                first_lo(item)

            def sequence(v, seq0, first=False, last=False):
                for q in range(PER_SEQ):
                    count = counter(v, seq0, q)
                    more = not (last and q == PER_SEQ - 1)
                    if q == 0 and not first:
                        next_lo(5, v, seq0)
                    for j in range(J):
                        if first and q == 0:
                            for item in FIRST_PIECES[j]:
                                first_lo(item)
                        if not more:
                            continue
                        if j == 2:
                            if q == PER_SEQ - 1:
                                pool.wait_ge(prof_loaded, 32 * (seq0 + 2) + (32 * v if not isinstance(v, int) else 0))
                            add_up_bias(count, 1)
                        for c in XSPLIT_AT.get(j, ()):
                            add_norm_bias(count, 1, (q + 1) % 2, c)
                        if j == RSTD_AT:
                            make_rstd(count, 1)
                        if q == 0 and not last and j == PROFILE_AT:
                            next_lo(0, v, seq0 + 1)
                            next_lo(1, v, seq0 + 1)
                        if q == PER_SEQ - 1 and j in EXPERT_AT:
                            next_lo(2 + EXPERT_AT[j], v, seq0 + 1)

            sequence(0, 0, first=True)
            with pool.Fori(0, BATCH - 2) as v:
                sequence(v, 1)
            sequence(0, BATCH - 1, last=True)


def kernel(x, itok_B_0_6, itok_B_0_15, L0_cond_down_w, L0_cond_down_b, L0_cond_up_w, L0_cond_up_b,
           L0_cond_ln_g, L0_cond_ln_b, L1_cond_fc1_w, L1_cond_fc1_b, L1_cond_fc2_w, L1_cond_fc2_b,
           L1_cond_experts_w, L1_cond_experts_b):
    import numpy as np
    import concourse.bacc as bacc
    from concourse import mybir as mb
    from concourse.bass_utils import run_bass_kernel_spmd

    a = {n: np.asarray(t) for n, t in dict(
        x=x, prof=itok_B_0_6, exp=itok_B_0_15, dw=L0_cond_down_w, db=L0_cond_down_b, uw=L0_cond_up_w,
        ub=L0_cond_up_b, g=L0_cond_ln_g, b=L0_cond_ln_b, w1=L1_cond_fc1_w, b1=L1_cond_fc1_b,
        w2=L1_cond_fc2_w, b2=L1_cond_fc2_b, we=L1_cond_experts_w, be=L1_cond_experts_b).items()}
    rows = a["x"].reshape(NBLK, P, T * D)
    cols = a["x"].reshape(NBLK, P, T, C, P).transpose(0, 4, 3, 2, 1).reshape(NBLK, P, C, TB)
    ins = {
        "x_rows_d": rows,
        "x_cols_d": cols,
        "itok_prof_d": a["prof"].reshape(1, BATCH),
        "itok_exp_d": a["exp"].reshape(1, BATCH),
        "down_w_d": a["dw"].reshape(NPROF, C, P, P).transpose(0, 2, 1, 3).reshape(NPROF, P, C * P),
        "up_w_d": a["uw"],
        "prof_vecs_d": np.concatenate([a["db"].reshape(NPROF, P, 1), a["g"].reshape(NPROF, C, P).transpose(0, 2, 1),
                                       a["b"].reshape(NPROF, C, P).transpose(0, 2, 1)], axis=2),
        "up_b_d": a["ub"],
        "w1_d": a["w1"].reshape(J, P, C, P).transpose(3, 0, 2, 1).reshape(P, J * C * P),
        "w2_d": a["w2"].reshape(SHARED, J, P).transpose(2, 1, 0).reshape(P, J * SHARED),
        "exp_w_d": a["we"].reshape(NEXP, P, J, P).transpose(0, 3, 2, 1).reshape(NEXP, P, J * P),
        "exp_b_d": a["be"].reshape(NEXP, P, 1),
        "const_vecs_d": np.concatenate([a["b1"].reshape(J, P).transpose(1, 0),
                                        a["b2"].reshape(SHARED // P, P).transpose(1, 0)], axis=1),
    }
    ins = {n: np.ascontiguousarray(t) for n, t in ins.items()}
    nc = bacc.Bacc("TRN2", target_bir_lowering=False, num_devices=1, dynamic_dma_scratch_size=1024)
    args = [nc.dram_tensor(n, t.shape, mb.dt.from_np(t.dtype), kind="ExternalInput").ap() for n, t in ins.items()]
    out = nc.dram_tensor("out_d", (NBLK, P, C, TB), mb.dt.float32, kind="ExternalOutput").ap()
    build(nc, *args, out)
    r = run_bass_kernel_spmd(nc, [ins], core_ids=[0])
    got = r.results[0]["out_d"]
    return got.reshape(NBLK, P, C, T, P).transpose(0, 4, 3, 2, 1).reshape(BATCH, SEQ, D)
```

```python
import concourse.bass as bass
from concourse import mybir
from contextlib import ExitStack

P = 128
BATCH, SEQ, D = 8, 1024, 512
NPROF, NEXP = 8, 16
HID, SHARED = 2048, 384
TB = 512
NBLK = BATCH * SEQ // TB
PER_SEQ = SEQ // TB
C = D // P
T = TB // P
J = HID // P
LAG = 2
PIECE = 512
STAGES = 3
Q = 32
NQ = P // Q
EXP_PIECES = HID * (D - SHARED) // P // PIECE
JQ = J // EXP_PIECES
EPS = 1e-5

XSPLIT_AT = {2: (0, 1), 4: (2,), 5: (3,)}
ROWS_AT = {3: 0, 4: 1, 5: 2, 6: 3}
DOWN_AT = {3: (0,), 4: (1,), 5: (2,), 6: (3,)}
Z_AT = 7
UP_AT = {8: (0, 1), 9: (2, 3)}
Y_AT = {8: (0, 1), 9: (2, 3)}
RSTD_AT = 9
NORM_AT = 10
EXCHANGE_AT = 11
X1_AT = {14: (0, 1), 15: (2, 3)}
PROFILE_AT = J - 1
EXPERT_AT = {6: 0, 10: 1, 14: 2}

AHEAD = 3


def _first_pieces():
    order = {-1: [("down", 0), ("up", 0)] + [("w1", n) for n in range(AHEAD)] + [("exp", 0), ("w2", 0)]}
    sent = 1
    for j in range(J):
        order[j] = [("w1", j + AHEAD)] if j + AHEAD < J else []
        if j % JQ == 2 and j // JQ + 1 < EXP_PIECES:
            order[j].append(("exp", j // JQ + 1))
        while sent * PIECE < min(j + 2, J) * SHARED:
            order[j].append(("w2", sent))
            sent += 1
    return order


FIRST_PIECES = _first_pieces()
FIRST_INDEX = {}
for _step in range(-1, J):
    for _item in FIRST_PIECES[_step]:
        FIRST_INDEX[_item] = len(FIRST_INDEX)
N_FIRST = len(FIRST_INDEX)
NEXT_ORDER = [("down", 0), ("up", 0), ("exp", 0), ("exp", 1), ("exp", 2), ("exp", 3)]


def build(nc, x, x_t, itok_prof, itok_exp, down_w, up_w, prof_vecs, up_b, w1, w2, exp_w,
          exp_b, const_vecs, out_t):
    fp32, fp32r = mybir.dt.float32, mybir.dt.float32r
    ALU, ACT = mybir.AluOpType, mybir.ActivationFunctionType
    ctx = ExitStack()
    with ctx:
        def sb(name, shape, dt=fp32):
            return ctx.enter_context(nc.sbuf_tensor(name, shape, dt))

        def sem(name):
            return ctx.enter_context(nc.semaphore(name))

        w1_s = sb("w1_s", [P, 2, J * C * P], fp32r)
        w2_s = sb("w2_s", [P, 2, J * SHARED], fp32r)
        exp_s = sb("exp_s", [P, 2, J * P], fp32r)
        down_s = sb("down_s", [P, 2, C * P], fp32r)
        up_s = sb("up_s", [P, 2, D], fp32r)
        stage = sb("stage", [P, STAGES, PIECE])
        x_rows = sb("x_rows", [P, T, D])
        turned = sb("turned", [P, C, NQ, T, Q])
        x_cols = sb("x_cols", [P, PER_SEQ, C, TB])
        xs = sb("xs", [P, 2, 2, TB], fp32r)
        x1_s = sb("x1_s", [P, 2, C, TB], fp32r)
        z_raw = sb("z_raw", [P, TB])
        h_raw = sb("h_raw", [P, 2, TB])
        h_s = sb("h_s", [P, 3, 2, TB], fp32r)
        prof_v = sb("prof_v", [P, 1 + 2 * C])
        bup = sb("bup", [P, D])
        const_v = sb("const_v", [P, J + SHARED // P])
        exp_v = sb("exp_v", [P, 1])
        ident = sb("ident", [P, P])
        stats = sb("stats", [P, T, 6])
        mean_var = sb("mean_var", [P, T, 2])
        var_eps = sb("var_eps", [P, T])
        rstd = sb("rstd", [P, T])
        neg_half = sb("neg_half", [P, T])
        eps = sb("eps", [P, T])
        warm = sb("warm", [P, 2])

        acc = [ctx.enter_context(nc.psum_tensor(f"acc{o}", [P, TB], fp32)) for o in range(C)]
        hid = [ctx.enter_context(nc.psum_tensor(f"hid{k}", [P, TB], fp32)) for k in range(2)]
        bank_a = ctx.enter_context(nc.psum_tensor("bank_a", [P, TB], fp32))
        bank_b = ctx.enter_context(nc.psum_tensor("bank_b", [P, TB], fp32))
        UP_BANK = [bank_b, bank_a, bank_b, bank_a]

        x_loaded, const_loaded = sem("x_loaded"), sem("const_loaded")
        xt_loaded = [sem(f"xt_loaded{c}") for c in range(C)]
        prof_loaded, exp_v_loaded = sem("prof_loaded"), sem("exp_v_loaded")
        stage_loaded = [sem(f"stage_loaded{s}") for s in range(STAGES)]
        out_stored = [sem(f"out_stored{o}") for o in range(C)]
        stage_hi, stage_split = sem("stage_hi"), sem("stage_split")
        const_set, ident_ready = sem("const_set"), sem("ident_ready")
        xb_ready, x_hi, x_split, xtb_ready = sem("xb_ready"), sem("x_hi"), sem("x_split"), sem("xtb_ready")
        down_done, z_done, z_hi, z_split = sem("down_done"), sem("z_done"), sem("z_hi"), sem("z_split")
        up_done, y_done, stats_done, aggr_done = sem("up_done"), sem("y_done"), sem("stats_done"), sem("aggr_done")
        var0_done, rstd0_done = sem("var0_done"), sem("rstd0_done")
        stats_seen, warm_set = sem("stats_seen"), sem("warm_set")
        var_done, rstd_done, norm_done, tr_done = sem("var_done"), sem("rstd_done"), sem("norm_done"), sem("tr_done")
        turned_done, exchanged = sem("turned_done"), sem("exchanged")
        x1_done, x1_hi, x1_split = sem("x1_done"), sem("x1_hi"), sem("x1_split")
        fc1_done, gelu_done, h_hi, h_split = sem("fc1_done"), sem("gelu_done"), sem("h_hi"), sem("h_split")
        fc2_done, acc_done, out_ready = sem("fc2_done"), sem("acc_done"), sem("out_ready")

        block = ctx.enter_context(nc.Block())

        def wait(eng, s, value):
            if not isinstance(value, int) or value > 0:
                eng.wait_ge(s, value)

        def plain(ap):
            return ap.bitcast(fp32)

        def piece_dst(kind, n, half):
            tensor = {"w1": w1_s, "w2": w2_s, "exp": exp_s, "down": down_s, "up": up_s}[kind]
            return tensor[:, half, n * PIECE:(n + 1) * PIECE]

        def next_index(m, v, seq0):
            return N_FIRST + len(NEXT_ORDER) * (seq0 - 1) + m + v * len(NEXT_ORDER)

        def stage_slot(m, seq0):
            return (N_FIRST + len(NEXT_ORDER) * (seq0 - 1) + m) % STAGES

        assert len(NEXT_ORDER) % STAGES == 0

        def stage_uses(m, v, seq0):
            return (N_FIRST + len(NEXT_ORDER) * (seq0 - 1) + m) // STAGES + 1 + v * (len(NEXT_ORDER) // STAGES)

        def counter(v, seq0, q):
            def count(per, n, shift=0):
                return per * (PER_SEQ * seq0 + q + shift) + n + v * (per * PER_SEQ)
            return count

        @block.sync
        def _(sp):
            def load_piece(slot, src):
                sp.dma_start(stage[:, slot, :], src).then_inc(stage_loaded[slot], 16)

            def source(kind, n, prof=None, expert=None):
                if kind == "w1":
                    return w1[:, n * PIECE:(n + 1) * PIECE]
                if kind == "w2":
                    return w2[:, n * PIECE:(n + 1) * PIECE]
                if kind == "exp":
                    return exp_w[bass.ds(expert, 1), :, n * PIECE:(n + 1) * PIECE].rearrange("e p n -> (e p) n")
                w = down_w if kind == "down" else up_w
                return w[bass.ds(prof, 1), :, :].rearrange("e p n -> (e p) n")

            def load_first(item):
                k = FIRST_INDEX[item]
                wait(sp, stage_split, k + 1 - STAGES)
                load_piece(k % STAGES, source(*item, prof0, expert0))

            def load_next(m, v, seq0, prof, expert):
                sp.wait_ge(stage_split, next_index(m, v, seq0) + 1 - STAGES)
                load_piece(stage_slot(m, seq0), source(*NEXT_ORDER[m], prof, expert))

            def load_profile(prof):
                sp.dma_start(prof_v[:], prof_vecs[bass.ds(prof, 1), :, :].rearrange("e p n -> (e p) n")).then_inc(prof_loaded, 16)
                sp.dma_start(bup[:], up_b[bass.ds(prof, 1), :].to_broadcast([P, D])).then_inc(prof_loaded, 16)

            def chosen(itok, n, most):
                return sp.value_load(itok[0:1, bass.ds(n, 1)], min_val=0, max_val=most)

            def block_rows(blk):
                return x[bass.ds(blk, 1), :, :].rearrange("b p n -> (b p) n").rearrange("p (t d) -> p t d", t=T)

            def exchange(count):
                sp.wait_ge(turned_done, count(T, T))
                for a in range(NQ):
                    for g in range(NQ):
                        sp.dma_start(x_rows[g * Q:(g + 1) * Q, :, a * T * Q:(a + 1) * T * Q],
                                     turned[a * Q:(a + 1) * Q, :, g, :, :].rearrange("p c t i -> p c (t i)"))\
                          .then_inc(exchanged, 16)

            def block_cols(tensor, blk, c):
                return tensor[bass.ds(blk, 1), :, c, :].rearrange("b p n -> (b p) n")

            prof0 = chosen(itok_prof, 0, NPROF - 1)
            load_piece(0, source("down", 0, prof0))
            load_profile(prof0)
            load_piece(1, source("up", 0, prof0))
            expert0 = chosen(itok_exp, 0, NEXP - 1)
            for item in FIRST_PIECES[-1][2:]:
                load_first(item)
            sp.dma_start(exp_v[:], exp_b[bass.ds(expert0, 1), :, :].rearrange("e p n -> (e p) n")).then_inc(exp_v_loaded, 16)

            def one_block(v, seq0, q, first, last, ids):
                count = counter(v, seq0, q)
                start = first and q == 0
                more = not (last and q == PER_SEQ - 1)
                blk = PER_SEQ * (seq0 + v) + q
                if q == 0:
                    ids["expert"] = chosen(itok_exp, seq0 + v, NEXP - 1) if not first else expert0
                    if not last:
                        ids["next_prof"] = chosen(itok_prof, seq0 + 1 + v, NPROF - 1)
                        ids["next_expert"] = chosen(itok_exp, seq0 + 1 + v, NEXP - 1)
                if not start:
                    for o in range(C):
                        sp.wait_ge(out_ready, count(C, o + 1, -1))
                        sp.dma_start(block_cols(out_t, blk - 1, o), x_cols[:, (q + 1) % 2, o, :]).then_inc(out_stored[o], 16)
                if more:
                    for c in range(C):
                        if not start:
                            sp.wait_ge(out_stored[c], count(16, 0))
                        sp.dma_start(x_cols[:, (q + 1) % 2, c, :], block_cols(x_t, blk + 1, c)).then_inc(xt_loaded[c], 16)
                    sp.wait_ge(x1_done, count(C, 0, 1))
                    sp.dma_start(x_rows[:], block_rows(blk + 1)).then_inc(x_loaded, 16)
                if q == 0 and not first:
                    sp.dma_start(exp_v[:], exp_b[bass.ds(ids["expert"], 1), :, :].rearrange("e p n -> (e p) n")).then_inc(exp_v_loaded, 16)

                def load_nexts(*pieces):
                    for m in pieces:
                        load_next(m, v, seq0 + 1, ids["next_prof"], ids["next_expert"])

                if q == 0 and not first and not last:
                    load_nexts(0, 1, 2)
                for j in range(J):
                    if start:
                        for item in FIRST_PIECES[j]:
                            load_first(item)
                    if more and j == EXCHANGE_AT:
                        exchange(count)
                if first and q == 0:
                    load_nexts(0, 1, 2)
                if not last:
                    load_nexts(*((3, 4) if q == 0 else (5,)))
                    if q == 0:
                        sp.wait_ge(x1_done, count(C, 0, 2))
                        load_profile(ids["next_prof"])

            def sequence(v, seq0, first=False, last=False):
                ids = {}
                for q in range(PER_SEQ):
                    one_block(v, seq0, q, first, last, ids)

            sequence(0, 0, first=True)
            with sp.Fori(0, BATCH - 2) as v:
                sequence(v, 1)
            sequence(0, BATCH - 1, last=True)
            for o in range(C):
                sp.wait_ge(out_ready, C * (NBLK - 1) + o + 1)
                sp.dma_start(block_cols(out_t, NBLK - 1, o), x_cols[:, (NBLK - 1) % 2, o, :]).then_inc(out_stored[o], 16)
            for o in range(C):
                sp.wait_ge(out_stored[o], 16 * NBLK)

        @block.tensor
        def _(pe):
            def three(out, w_hi, w_lo, m_hi, m_lo, start, stop):
                nc.tensor.matmul(out, w_hi, m_hi, start=start, stop=False)
                nc.tensor.matmul(out, w_hi, m_lo, start=False, stop=False)
                return nc.tensor.matmul(out, w_lo, m_hi, start=False, stop=stop)

            def down(count, shift, c, weights, x_hi_lo=None):
                if c == 0:
                    wait(pe, x1_done, count(C, 0, shift))
                    if weights is not None:
                        pe.wait_ge(stage_split, weights)
                pe.wait_ge(x_split, count(C, c + 1, shift))
                k = slice(c * P, (c + 1) * P)
                part = x_hi_lo or (xs[:, c % 2, 0, :], xs[:, c % 2, 1, :])
                three(bank_a[:], down_s[:, 0, k], down_s[:, 1, k], *part, c == 0, c == C - 1).then_inc(down_done, 1)

            def up(count, shift, t, weights):
                if t == 0:
                    pe.wait_ge(z_split, count(1, 1, shift))
                    if weights is not None:
                        pe.wait_ge(stage_split, weights)
                if t >= 2:
                    pe.wait_ge(y_done, count(T, t - 1, shift))
                k = slice(t * P, (t + 1) * P)
                three(UP_BANK[t][:], xs[:, 0, 0, k], xs[:, 0, 1, k], up_s[:, 0, :], up_s[:, 1, :],
                      True, True).then_inc(up_done, 1)

            def transpose(t):
                pe.wait_ge(norm_done, t + 1)
                for c in range(C):
                    columns = acc[c][:].rearrange("p (a t i) -> p a t i", a=NQ, t=T)
                    ins = nc.tensor.transpose(columns[:, :, t, :], x_rows[:, t, c * P:(c + 1) * P], ident[:])
                    if t == T - 1:
                        ins.then_inc(tr_done, 1)

            def fc1(count, j, start_block):
                wait(pe, gelu_done, count(J, j - 1))
                if start_block:
                    pe.wait_ge(stage_split, FIRST_INDEX[("w1", j)] + 1)
                for c in range(C):
                    if j == 0:
                        pe.wait_ge(x1_split, count(C, c + 1))
                    k = slice((j * C + c) * P, (j * C + c + 1) * P)
                    ins = three(hid[j % 2][:], w1_s[:, 0, k], w1_s[:, 1, k], x1_s[:, 0, c, :], x1_s[:, 1, c, :],
                                c == 0, c == C - 1)
                ins.then_inc(fc1_done, 1)

            def fc2(count, j, start_block, weights):
                pe.wait_ge(h_split, count(J, j + 1))
                if start_block:
                    last = (("w2", ((j + 1) * SHARED - 1) // PIECE), ("exp", j // JQ))
                    pe.wait_ge(stage_split, max(FIRST_INDEX[i] for i in last) + 1)
                elif weights is not None and j % JQ == 0:
                    pe.wait_ge(stage_split, weights[j // JQ])
                for o in range(C):
                    if j == 0:
                        wait(pe, out_ready, count(C, o + 1, -1))
                    if o < SHARED // P:
                        k = slice(j * SHARED + o * P, j * SHARED + (o + 1) * P)
                        w_hi, w_lo = w2_s[:, 0, k], w2_s[:, 1, k]
                    else:
                        k = slice(j * P, (j + 1) * P)
                        w_hi, w_lo = exp_s[:, 0, k], exp_s[:, 1, k]
                    ins = three(acc[o][:], w_hi, w_lo, h_s[:, j % 3, 0, :], h_s[:, j % 3, 1, :], j == 0, j == J - 1)
                    if j == J - 1:
                        ins.then_inc(acc_done, 1)
                if j < J - 1:
                    ins.then_inc(fc2_done, 1)

            zero = counter(0, 0, 0)
            for c in range(C):
                down(zero, 0, c, FIRST_INDEX[("down", 0)] + 1, (x1_s[:, 0, c, :], x1_s[:, 1, c, :]))
            for t in range(T):
                up(zero, 0, t, FIRST_INDEX[("up", 0)] + 1)
            pe.wait_ge(ident_ready, 1)
            for t in range(T):
                transpose(t)

            def sequence(v, seq0, first=False, last=False):
                for q in range(PER_SEQ):
                    count = counter(v, seq0, q)
                    start_block = first and q == 0
                    more = not (last and q == PER_SEQ - 1)
                    new_profile = more and q == PER_SEQ - 1
                    down_w_at = next_index(0, v, seq0 + 1) + 1 if new_profile else None
                    up_w_at = next_index(1, v, seq0 + 1) + 1 if new_profile else None
                    exp_at = [next_index(2 + n, v, seq0) + 1 for n in range(EXP_PIECES)] if q == 0 and not first else None
                    for j in range(J):
                        fc1(count, j, start_block)
                        if j >= LAG:
                            fc2(count, j - LAG, start_block, exp_at)
                        if more:
                            for c in DOWN_AT.get(j, ()):
                                down(count, 1, c, down_w_at)
                            for t in UP_AT.get(j, ()):
                                up(count, 1, t, up_w_at)
                    for j in range(J - LAG, J):
                        fc2(count, j, start_block, exp_at)

            sequence(0, 0, first=True)
            with pe.Fori(0, BATCH - 2) as v:
                sequence(v, 1)
            sequence(0, BATCH - 1, last=True)

        @block.scalar
        def _(act):
            def piece_hi(kind, n, slot, uses):
                act.wait_ge(stage_loaded[slot], uses * 16)
                nc.scalar.activation(piece_dst(kind, n, 0), stage[:, slot, :], ACT.Copy).then_inc(stage_hi, 1)

            def first_hi(item):
                k = FIRST_INDEX[item]
                piece_hi(*item, k % STAGES, k // STAGES + 1)

            def next_hi(m, v, seq0):
                piece_hi(*NEXT_ORDER[m], stage_slot(m, seq0), stage_uses(m, v, seq0))

            def split_x(count, shift, q, c):
                act.wait_ge(xt_loaded[c], count(16, 16, shift))
                if c == 0:
                    wait(act, up_done, count(T, 0, shift))
                elif c == 1:
                    wait(act, down_done, count(C, 0, shift))
                else:
                    act.wait_ge(down_done, count(C, c - 1, shift))
                nc.scalar.activation(xs[:, c % 2, 0, :], x_cols[:, q, c, :], ACT.Copy).then_inc(x_hi, 1)

            def relu_z(count, shift):
                act.wait_ge(down_done, count(C, C, shift))
                wait(act, z_split, count(1, 0, shift))
                nc.scalar.activation(z_raw[:].rearrange("p (t a i) -> p a t i", t=T, a=NQ),
                                     bank_a[:].rearrange("p (a t i) -> p a t i", a=NQ, t=T),
                                     ACT.Relu, bias=prof_v[:, 0:1]).then_inc(z_done, 1)

            def add_norm_bias(count, shift, q, c):
                act.wait_ge(x_split, count(C, c + 1, shift))
                nc.scalar.activation(x_cols[:, q, c, :], x_cols[:, q, c, :], ACT.Identity,
                                     bias=prof_v[:, 1 + C + c:2 + C + c]).then_inc(xtb_ready, 1)

            def split_x1(count, shift, q):
                for c in range(C):
                    act.wait_ge(x1_done, count(C, c + 1, shift))
                    nc.scalar.activation(x1_s[:, 0, c, :], x_cols[:, q, c, :], ACT.Copy).then_inc(x1_hi, 1)

            act.dma_start(x_cols[:, 0, 0, :], x_t[0, :, 0, :]).then_inc(xt_loaded[0], 16)
            act.wait_ge(warm_set, 1)
            nc.scalar.activation(warm[:, 1:2], warm[:, 0:1], ACT.Gelu)
            for c in range(1, C):
                act.dma_start(x_cols[:, 0, c, :], x_t[0, :, c, :]).then_inc(xt_loaded[c], 16)
            act.dma_start(const_v[:], const_vecs).then_inc(const_loaded, 16)
            act.dma_start(x_rows[:], x[0, :, :].rearrange("p (t d) -> p t d", t=T)).then_inc(x_loaded, 16)
            zero = counter(0, 0, 0)
            for c in range(C):
                if c == 1:
                    first_hi(("down", 0))
                act.wait_ge(xt_loaded[c], 16)
                nc.scalar.activation(x1_s[:, 0, c, :], x_cols[:, 0, c, :], ACT.Copy).then_inc(x_hi, 1)
            first_hi(("up", 0))
            act.wait_ge(prof_loaded, 32)
            relu_z(zero, 0)
            for c in range(C):
                add_norm_bias(zero, 0, 0, c)
            for item in FIRST_PIECES[-1][2:]:
                first_hi(item)
            act.wait_ge(const_loaded, 16)
            split_x1(zero, 0, 0)

            def sequence(v, seq0, first=False, last=False):
                for q in range(PER_SEQ):
                    count = counter(v, seq0, q)
                    more = not (last and q == PER_SEQ - 1)
                    for j in range(J):
                        act.wait_ge(fc1_done, count(J, j + 1))
                        wait(act, h_split, count(J, j - 1))
                        nc.scalar.activation(h_raw[:, j % 2, :], hid[j % 2][:], ACT.Gelu,
                                             bias=const_v[:, j:j + 1]).then_inc(gelu_done, 1)
                        if first and q == 0:
                            for item in FIRST_PIECES[j]:
                                first_hi(item)
                        if j == 0 and q == 0 and not first:
                            act.wait_ge(acc_done, count(C, 0))
                            next_hi(5, v, seq0)
                        if not more:
                            continue
                        for c in XSPLIT_AT.get(j, ()):
                            split_x(count, 1, (q + 1) % 2, c)
                        if j == Z_AT:
                            if q == PER_SEQ - 1:
                                act.wait_ge(prof_loaded, 32 * (seq0 + 2) + v * 32)
                            relu_z(count, 1)
                            for c in range(C):
                                add_norm_bias(count, 1, (q + 1) % 2, c)
                        if q == 0 and not last and j == PROFILE_AT:
                            act.wait_ge(down_done, count(C, 0, 2))
                            next_hi(0, v, seq0 + 1)
                            act.wait_ge(up_done, count(T, 0, 2))
                            next_hi(1, v, seq0 + 1)
                        if q == PER_SEQ - 1 and j in EXPERT_AT:
                            n = EXPERT_AT[j]
                            act.wait_ge(fc2_done, count(J - 1, (n + 1) * JQ))
                            next_hi(2 + n, v, seq0 + 1)
                    if more:
                        split_x1(count, 1, (q + 1) % 2)

            sequence(0, 0, first=True)
            with act.Fori(0, BATCH - 2) as v:
                sequence(v, 1)
            sequence(0, BATCH - 1, last=True)

        @block.vector
        def _(dve):
            def split_x(count, shift, q, c):
                dve.wait_ge(x_hi, count(C, c + 1, shift))
                nc.vector.tensor_tensor(xs[:, c % 2, 1, :], x_cols[:, q, c, :], plain(xs[:, c % 2, 0, :]),
                                        ALU.subtract).then_inc(x_split, 1)

            def split_z(count, shift):
                dve.wait_ge(z_done, count(1, 1, shift))
                nc.vector.tensor_copy(xs[:, 0, 0, :], z_raw[:]).then_inc(z_hi, 1)
                dve.wait_ge(z_hi, count(1, 1, shift))
                nc.vector.tensor_tensor(xs[:, 0, 1, :], z_raw[:], plain(xs[:, 0, 0, :]),
                                        ALU.subtract).then_inc(z_split, 1)

            def residual_stats(count, shift, t):
                dve.wait_ge(xb_ready, count(T, t + 1, shift))
                dve.wait_ge(up_done, count(T, t + 1, shift))
                nc.vector.tensor_tensor(x_rows[:, t, :], UP_BANK[t][:], x_rows[:, t, :], ALU.add).then_inc(y_done, 1)
                dve.wait_ge(y_done, count(T, t + 1, shift))
                nc.vector.bn_stats(stats[:, t, :], x_rows[:, t, :]).then_inc(stats_done, 1)
                dve.wait_ge(stats_done, count(T, t + 1, shift))
                dve.sem_inc(stats_seen)
                nc.vector.bn_aggr(mean_var[:, t, :], stats[:, t, :]).then_inc(aggr_done, 1)

            def norm(count, shift):
                dve.wait_ge(rstd_done, count(1, 0, shift))
                for t in range(T):
                    norm_tile(t)

            def norm_tile(t):
                nc.vector.tensor_scalar(x_rows[:, t, :], x_rows[:, t, :], mean_var[:, t, 0:1], rstd[:, t:t + 1],
                                        ALU.subtract, ALU.mult).then_inc(norm_done, 1)

            def turn(count, shift):
                for t in range(T):
                    dve.wait_ge(norm_done, count(T, t + 1, shift))
                    nc.vector.transpose(turned[:, :, :, t, :].rearrange("p c g i -> p (c g) i"),
                                        x_rows[:, t, :].rearrange("p (k i) -> p k i", i=Q)).then_inc(turned_done, 1)

            def make_x1(count, shift, q, c, normed):
                dve.wait_ge(xtb_ready, count(C, c + 1, shift))
                nc.vector.scalar_tensor_tensor(out=x_cols[:, q, c, :], in0=normed, scalar=prof_v[:, 1 + c:2 + c],
                                               in1=x_cols[:, q, c, :], op0=ALU.mult, op1=ALU.add).then_inc(x1_done, 1)

            def split_x1(count, shift, q, c):
                dve.wait_ge(x1_hi, count(C, c + 1, shift))
                nc.vector.tensor_tensor(x1_s[:, 1, c, :], x_cols[:, q, c, :], plain(x1_s[:, 0, c, :]),
                                        ALU.subtract).then_inc(x1_split, 1)

            zero = counter(0, 0, 0)
            nc.vector.memset(warm[:], 0.0).then_inc(warm_set, 1)
            for c in range(C):
                if c == 1:
                    dve.wait_ge(stage_hi, 1)
                    nc.vector.tensor_tensor(down_s[:, 1, :], stage[:, 0, :], plain(down_s[:, 0, :]),
                                            ALU.subtract).then_inc(stage_split, 1)
                dve.wait_ge(x_hi, c + 1)
                nc.vector.tensor_tensor(x1_s[:, 1, c, :], x_cols[:, 0, c, :], plain(x1_s[:, 0, c, :]),
                                        ALU.subtract).then_inc(x_split, 1)
            dve.wait_ge(x_loaded, 16)
            dve.wait_ge(prof_loaded, 32)
            for t in range(T):
                if t == T // 2:
                    split_z(zero, 0)
                nc.vector.tensor_tensor(x_rows[:, t, :], x_rows[:, t, :], bup[:], ALU.add).then_inc(xb_ready, 1)
            for t in range(T + 1):
                if t < T:
                    residual_stats(zero, 0, t)
                if t > 0:
                    dve.wait_ge(rstd0_done, t)
                    norm_tile(t - 1)
            for c in range(C + 1):
                if c < C:
                    dve.wait_ge(tr_done, c + 1)
                    make_x1(zero, 0, 0, c, acc[c][:])
                if c > 0:
                    split_x1(zero, 0, 0, c - 1)
            dve.wait_ge(const_loaded, 16)

            def sequence(v, seq0, first=False, last=False):
                for q in range(PER_SEQ):
                    count = counter(v, seq0, q)
                    more = not (last and q == PER_SEQ - 1)
                    for j in range(J):
                        dve.wait_ge(gelu_done, count(J, j + 1))
                        if j >= 3:
                            dve.wait_ge(fc2_done, count(J - 1, j - 2))
                        hi, lo = h_s[:, j % 3, 0, :], h_s[:, j % 3, 1, :]
                        nc.vector.tensor_copy(hi, h_raw[:, j % 2, :]).then_inc(h_hi, 1)
                        dve.wait_ge(h_hi, count(J, j + 1))
                        nc.vector.tensor_tensor(lo, h_raw[:, j % 2, :], plain(hi), ALU.subtract).then_inc(h_split, 1)
                        if not more:
                            continue
                        for c in XSPLIT_AT.get(j, ()):
                            split_x(count, 1, (q + 1) % 2, c)
                        if j == Z_AT:
                            split_z(count, 1)
                        for t in Y_AT.get(j, ()):
                            residual_stats(count, 1, t)
                        if j == NORM_AT:
                            norm(count, 1)
                            turn(count, 1)
                        for c in X1_AT.get(j, ()):
                            dve.wait_ge(exchanged, count(16 * NQ * NQ, 0, 1))
                            make_x1(count, 1, (q + 1) % 2, c, x_rows[:, c, :])
                    if more:
                        for c in range(C):
                            split_x1(count, 1, (q + 1) % 2, c)
                    if q == 0:
                        dve.wait_ge(exp_v_loaded, 16 * (seq0 + 1) + v * 16)
                    for o in range(C):
                        bias = const_v[:, J + o:J + o + 1] if o < SHARED // P else exp_v[:]
                        dve.wait_ge(acc_done, count(C, o + 1))
                        nc.vector.scalar_tensor_tensor(out=x_cols[:, q, o, :], in0=acc[o][:], scalar=bias,
                                                       in1=x_cols[:, q, o, :], op0=ALU.add, op1=ALU.add).then_inc(out_ready, 1)

            sequence(0, 0, first=True)
            with dve.Fori(0, BATCH - 2) as v:
                sequence(v, 1)
            sequence(0, BATCH - 1, last=True)

        @block.gpsimd
        def _(pool):
            def piece_lo(kind, n, slot, index):
                pool.wait_ge(stage_hi, index + 1)
                nc.gpsimd.tensor_tensor(piece_dst(kind, n, 1), stage[:, slot, :], plain(piece_dst(kind, n, 0)),
                                        ALU.subtract).then_inc(stage_split, 1)

            def first_lo(item):
                k = FIRST_INDEX[item]
                piece_lo(*item, k % STAGES, k)

            def next_lo(m, v, seq0):
                piece_lo(*NEXT_ORDER[m], stage_slot(m, seq0), next_index(m, v, seq0))

            def add_up_bias(count, shift, t):
                pool.wait_ge(x_loaded, count(16, 16, shift))
                nc.gpsimd.tensor_tensor(x_rows[:, t, :], x_rows[:, t, :], bup[:], ALU.add).then_inc(xb_ready, 1)

            def make_rstd(count, shift):
                pool.wait_ge(aggr_done, count(T, T, shift))
                wait(pool, norm_done, count(T, 0, shift))
                nc.gpsimd.tensor_tensor(var_eps[:], mean_var[:, :, 1], eps[:], ALU.add).then_inc(var_done, 1)
                pool.wait_ge(var_done, count(1, 0, shift))
                nc.gpsimd.tensor_tensor(rstd[:], var_eps[:], neg_half[:], ALU.pow).then_inc(rstd_done, 1)

            nc.gpsimd.memset(neg_half[:], -0.5).then_inc(const_set, 1)
            nc.gpsimd.memset(eps[:], EPS).then_inc(const_set, 1)
            nc.gpsimd.memset(ident[:], 0.0).then_inc(const_set, 1)
            pool.wait_ge(const_set, 3)
            nc.gpsimd.affine_select(out=ident[:], in_=ident[:], compare_op=ALU.not_equal, fill=1.0, base=0,
                                    pattern=[[-1, P]], channel_multiplier=1).then_inc(ident_ready, 1)
            pool.wait_ge(stage_split, 1)
            first_lo(("up", 0))
            zero = counter(0, 0, 0)
            pool.wait_ge(prof_loaded, 32)
            for item in FIRST_PIECES[-1][2:4]:
                first_lo(item)
            for t in range(T):
                one = slice(t, t + 1)
                pool.wait_ge(aggr_done, t + 1)
                nc.gpsimd.tensor_tensor(var_eps[:, one], mean_var[:, one, 1], eps[:, one], ALU.add).then_inc(var0_done, 1)
                pool.wait_ge(var0_done, t + 1)
                nc.gpsimd.tensor_tensor(rstd[:, one], var_eps[:, one], neg_half[:, one], ALU.pow).then_inc(rstd0_done, 1)
            for item in FIRST_PIECES[-1][4:]:
                first_lo(item)

            def sequence(v, seq0, first=False, last=False):
                for q in range(PER_SEQ):
                    count = counter(v, seq0, q)
                    more = not (last and q == PER_SEQ - 1)
                    if q == 0 and not first:
                        next_lo(5, v, seq0)
                    for j in range(J):
                        if first and q == 0:
                            for item in FIRST_PIECES[j]:
                                first_lo(item)
                        if not more:
                            continue
                        if j in ROWS_AT:
                            if q == PER_SEQ - 1 and ROWS_AT[j] == 0:
                                pool.wait_ge(prof_loaded, 32 * (seq0 + 2) + v * 32)
                            add_up_bias(count, 1, ROWS_AT[j])
                        if j == RSTD_AT:
                            make_rstd(count, 1)
                        if q == 0 and not last and j == PROFILE_AT:
                            next_lo(0, v, seq0 + 1)
                            next_lo(1, v, seq0 + 1)
                        if q == PER_SEQ - 1 and j in EXPERT_AT:
                            next_lo(2 + EXPERT_AT[j], v, seq0 + 1)

            sequence(0, 0, first=True)
            with pool.Fori(0, BATCH - 2) as v:
                sequence(v, 1)
            sequence(0, BATCH - 1, last=True)


def kernel(x, itok_B_0_6, itok_B_0_15, L0_cond_down_w, L0_cond_down_b, L0_cond_up_w, L0_cond_up_b,
           L0_cond_ln_g, L0_cond_ln_b, L1_cond_fc1_w, L1_cond_fc1_b, L1_cond_fc2_w, L1_cond_fc2_b,
           L1_cond_experts_w, L1_cond_experts_b):
    import numpy as np
    import concourse.bacc as bacc
    from concourse import mybir as mb
    from concourse.bass_utils import run_bass_kernel_spmd

    a = {n: np.asarray(t) for n, t in dict(
        x=x, prof=itok_B_0_6, exp=itok_B_0_15, dw=L0_cond_down_w, db=L0_cond_down_b, uw=L0_cond_up_w,
        ub=L0_cond_up_b, g=L0_cond_ln_g, b=L0_cond_ln_b, w1=L1_cond_fc1_w, b1=L1_cond_fc1_b,
        w2=L1_cond_fc2_w, b2=L1_cond_fc2_b, we=L1_cond_experts_w, be=L1_cond_experts_b).items()}
    rows = a["x"].reshape(NBLK, P, T * D)
    cols = a["x"].reshape(NBLK, NQ, Q, T, C, P).transpose(0, 5, 4, 1, 3, 2).reshape(NBLK, P, C, TB)
    ins = {
        "x_rows_d": rows,
        "x_cols_d": cols,
        "itok_prof_d": a["prof"].reshape(1, BATCH),
        "itok_exp_d": a["exp"].reshape(1, BATCH),
        "down_w_d": a["dw"].reshape(NPROF, C, P, P).transpose(0, 2, 1, 3).reshape(NPROF, P, C * P),
        "up_w_d": a["uw"],
        "prof_vecs_d": np.concatenate([a["db"].reshape(NPROF, P, 1), a["g"].reshape(NPROF, C, P).transpose(0, 2, 1),
                                       a["b"].reshape(NPROF, C, P).transpose(0, 2, 1)], axis=2),
        "up_b_d": a["ub"],
        "w1_d": a["w1"].reshape(J, P, C, P).transpose(3, 0, 2, 1).reshape(P, J * C * P),
        "w2_d": a["w2"].reshape(SHARED, J, P).transpose(2, 1, 0).reshape(P, J * SHARED),
        "exp_w_d": a["we"].reshape(NEXP, P, J, P).transpose(0, 3, 2, 1).reshape(NEXP, P, J * P),
        "exp_b_d": a["be"].reshape(NEXP, P, 1),
        "const_vecs_d": np.concatenate([a["b1"].reshape(J, P).transpose(1, 0),
                                        a["b2"].reshape(SHARED // P, P).transpose(1, 0)], axis=1),
    }
    ins = {n: np.ascontiguousarray(t) for n, t in ins.items()}
    nc = bacc.Bacc("TRN2", target_bir_lowering=False, num_devices=1, dynamic_dma_scratch_size=1024)
    args = [nc.dram_tensor(n, t.shape, mb.dt.from_np(t.dtype), kind="ExternalInput").ap() for n, t in ins.items()]
    out = nc.dram_tensor("out_d", (NBLK, P, C, TB), mb.dt.float32, kind="ExternalOutput").ap()
    build(nc, *args, out)
    r = run_bass_kernel_spmd(nc, [ins], core_ids=[0])
    got = r.results[0]["out_d"]
    return got.reshape(NBLK, P, C, NQ, T, Q).transpose(0, 3, 5, 4, 2, 1).reshape(BATCH, SEQ, D)
```
